# Optimizing a Trainium2 kernel written in Bass

```python
import numpy as np
import jax
import jax.numpy as jnp

def _softmax(x, axis=-1):
    return jax.nn.softmax(x, axis=axis)

def _gelu(x):
    return jax.nn.gelu(x, approximate=True)

def _silu(x):
    return jax.nn.silu(x)

def _sigmoid(x):
    return jax.nn.sigmoid(x)

def _layernorm(x, axis=-1, eps=1e-05):
    m = jnp.mean(x, axis=axis, keepdims=True)
    v = jnp.var(x, axis=axis, keepdims=True)
    return (x - m) / jnp.sqrt(v + eps)

def _scatter_add(tgt, idx, src, axis=0):
    return tgt.at[idx].add(src)

def _segment_sum(src, seg, n):
    return jax.ops.segment_sum(src, seg, n)
kernel_name = 'mk_gnn_preln_d1_gnn_r64_6adb9f'

def setup_inputs(seed: int=0):
    np.random.seed(seed)
    _w = jnp.asarray

    def _rec_inputs():
        import jax
        import jax.numpy as jnp
        _gk = jax.random.key(seed)
        x = -0.000202 + 1 * jax.random.normal(jax.random.fold_in(_gk, 1), (50000, 128), jnp.float32)
        src = jax.random.randint(jax.random.fold_in(_gk, 2), (12500,), 0, 50000, jnp.int32)
        dst = jax.random.randint(jax.random.fold_in(_gk, 3), (12500,), 0, 50000, jnp.int32)
        _o = jnp.argsort(dst, stable=True)
        src = src[_o]
        dst = dst[_o]
        return (x, src, dst)
    x, src, dst = _rec_inputs()

    def _L0_gnn_setup():
        import jax, jax.numpy as jnp
        import numpy as np
        N, E, D_IN, H, D_OUT = (50000, 25000, 128, 512, 128)

        def _gin_agg(x, edge_index):
            src, dst = (edge_index[0], edge_index[1])
            return x + jax.ops.segment_sum(x[src], dst, num_segments=N)
        key = jax.random.key(seed)
        ks = jax.random.split(key, 10)
        feature = jax.random.normal(ks[0], (N, D_IN), dtype=jnp.float32)
        edge_index = jax.random.randint(ks[1], (2, E), 0, N, dtype=jnp.int64)

        def lin(k, fan_in, fan_out):
            kw, kb = jax.random.split(k)
            bound = 1.0 / np.sqrt(fan_in)
            w = jax.random.uniform(kw, (fan_in, fan_out), jnp.float32, -bound, bound)
            b = jax.random.uniform(kb, (fan_out,), jnp.float32, -bound, bound)
            return (w, b)
        w1, b1 = lin(ks[2], D_IN, H)
        w2, b2 = lin(ks[3], H, H)
        w3, b3 = lin(ks[4], H, H)
        w4, b4 = lin(ks[5], H, D_OUT)
        return {'feature': feature, 'edge_index': edge_index, 'w1': w1, 'b1': b1, 'w2': w2, 'b2': b2, 'w3': w3, 'b3': b3, 'w4': w4, 'b4': b4}
    _L0_gnn_all = _L0_gnn_setup()
    _L0_gnn_in = {k: v for k, v in _L0_gnn_all.items() if k in ('w1', 'b1', 'w2', 'b2', 'w3', 'b3', 'w4', 'b4')}
    del _L0_gnn_all
    return {'x': x, 'src': src, 'dst': dst, 'L0_gnn_w1': _L0_gnn_in['w1'], 'L0_gnn_b1': _L0_gnn_in['b1'], 'L0_gnn_w2': _L0_gnn_in['w2'], 'L0_gnn_b2': _L0_gnn_in['b2'], 'L0_gnn_w3': _L0_gnn_in['w3'], 'L0_gnn_b3': _L0_gnn_in['b3'], 'L0_gnn_w4': _L0_gnn_in['w4'], 'L0_gnn_b4': _L0_gnn_in['b4']}

def reference(x, src, dst, L0_gnn_w1, L0_gnn_b1, L0_gnn_w2, L0_gnn_b2, L0_gnn_w3, L0_gnn_b3, L0_gnn_w4, L0_gnn_b4):
    import jax
    import jax.numpy as jnp

    def _L0_gnn_ref(feature, edge_index, w1, b1, w2, b2, w3, b3, w4, b4):
        import jax, jax.numpy as jnp
        import numpy as np
        N, E, D_IN, H, D_OUT = (50000, 25000, 128, 512, 128)

        def _gin_agg(x, edge_index):
            src, dst = (edge_index[0], edge_index[1])
            return x + jax.ops.segment_sum(x[src], dst, num_segments=N)
        h = _gin_agg(feature, edge_index)
        h = jnp.maximum(h @ w1 + b1, 0.0) @ w2 + b2
        h = jax.nn.elu(h)
        h2 = _gin_agg(h, edge_index)
        out = jnp.maximum(h2 @ w3 + b3, 0.0) @ w4 + b4
        return out
    edge_index = jnp.stack([src, dst])
    h = jnp.maximum(_layernorm(x, axis=-1), 0.0)
    x = x + _L0_gnn_ref(h, edge_index, L0_gnn_w1, L0_gnn_b1, L0_gnn_w2, L0_gnn_b2, L0_gnn_w3, L0_gnn_b3, L0_gnn_w4, L0_gnn_b4)
    return x

_drawn_inputs = setup_inputs


def setup_inputs(seed=0):
    import zlib

    import numpy as np

    out = dict(_drawn_inputs(seed))
    spreads = {}
    factors = {'L0_gnn_b1': 8.0, 'L0_gnn_b2': 7.789, 'L0_gnn_b3': 5.893}
    for name, (base, spread) in spreads.items():
        noise = np.random.default_rng([zlib.crc32(name.encode()), seed]).standard_normal(out[name].shape)
        drawn = base * np.exp(spread * noise) if base else spread * noise
        out[name] = jnp.asarray(drawn.astype(out[name].dtype))
    for name, factor in factors.items():
        out[name] = (out[name] * factor).astype(out[name].dtype)
    return out
```

```python
from contextlib import ExitStack

import concourse.bass as bass
from concourse import mybir

P = 128
ROWS = 512
SUB = ROWS // P
EPS = 1e-5
F32 = mybir.dt.float32
F32R = mybir.dt.float32r
I32 = mybir.dt.int32
ALU = mybir.AluOpType
ACT = mybir.ActivationFunctionType


def wait(engine, sem, value):
    if isinstance(value, int) and value <= 0:
        return
    engine.wait_ge(sem, value)


def gnn_kernel(nc, x, src, dst, w1, b1, w2, b2, w3, b3, w4, b4, out):
    N, D = x.shape
    E = src.shape[0]
    H = w1.shape[1]
    KC = H // P
    T = -(-N // ROWS)
    TE = -(-E // P)
    TE2 = TE + TE % 2
    TE4 = (TE + 2 + 3) // 4 * 4
    LAST_E = E - (TE - 1) * P
    TRASH = N
    SUM_ROWS = -(-(N + P) // P) * P
    E0 = 6
    assert D == P and H % P == 0 and SUB == KC == 4 and TE4 <= P and T >= 8 and TE4 >= 20

    z_table = nc.dram_tensor("z_table", [N, H], F32).ap()
    z_sums = nc.dram_tensor("z_sums", [SUM_ROWS, H], F32).ap()
    agg_table = nc.dram_tensor("agg_table", [SUM_ROWS, D], F32).ap()
    key_rows = nc.dram_tensor("key_rows", [TE4 * P], F32).ap()
    win_rows = nc.dram_tensor("win_rows", [TE4 * P], F32).ap()

    ctx = ExitStack()
    with ctx:
        def sb(name, shape, dt=F32):
            return ctx.enter_context(nc.sbuf_tensor(name, shape, dt))

        def sem(name):
            return ctx.enter_context(nc.semaphore(name))

        w_hi = {n: sb(f"w{n}_hi", [P, s], F32R) for n, s in ((1, H), (2, KC * H), (3, KC * H), (4, KC * D))}
        w_lo = {n: sb(f"w{n}_lo", [P, s], F32R) for n, s in ((1, H), (2, KC * H), (3, KC * H), (4, KC * D))}
        NB = 2 * KC + 1
        b_nat = sb("b_nat", [NB, P])
        b_cols = sb("b_cols", [P, NB])
        b1_col, b2_col, b4_col = b_cols[:, 0:KC], b_cols[:, KC:2 * KC], b_cols[:, 2 * KC:NB]
        b3_row = sb("b3_row", [P, H])
        b4_row = sb("b4_row", [P, D])
        ident = sb("ident", [P, P])
        upper = sb("upper", [P, P])
        ones = sb("ones", [P, P])
        zeros = sb("zeros", [P, ROWS])

        x_in = sb("x_in", [P, 2, SUB * D])
        agg_in = sb("agg_in", [P, 2, SUB * D])
        h0 = sb("h0", [P, 2, SUB * D])
        hT_hi = sb("hT_hi", [P, ROWS], F32R)
        hT_lo = sb("hT_lo", [P, ROWS], F32R)
        a1 = sb("a1", [P, KC, ROWS])
        a1_hi = sb("a1_hi", [P, KC, ROWS], F32R)
        a1_lo = sb("a1_lo", [P, KC, ROWS], F32R)
        pre2 = sb("pre2", [P, 2, ROWS])
        ex2 = sb("ex2", [P, 2, ROWS])
        h2 = sb("h2", [P, 2, ROWS])
        h2_hi = sb("h2_hi", [P, KC, ROWS], F32R)
        h2_lo = sb("h2_lo", [P, KC, ROWS], F32R)
        z_out = sb("z_out", [P, 2, SUB * H])
        z_b3 = sb("z_b3", [P, SUB * H])
        a3_hi = sb("a3_hi", [P, KC, ROWS], F32R)
        a3_lo = sb("a3_lo", [P, KC, ROWS], F32R)
        oT = sb("oT", [P, ROWS])
        x_res = sb("x_res", [P, 2, SUB * D])
        bn = sb("bn", [P, SUB, 6])
        mv = sb("mv", [P, 2, SUB, 2])
        rstd = sb("rstd", [P, 2, SUB])
        nmr = sb("nmr", [P, 2, SUB])

        key_all = sb("key_all", [P, TE4])
        win_all = sb("win_all", [P, TE4])
        edge_no = sb("edge_no", [P, TE4])
        src_f = sb("src_f", [P, TE4])
        src_all = sb("src_all", [P, TE4], I32)
        dst_all = sb("dst_all", [P, TE4], I32)
        from_all = sb("from_all", [P, TE4], I32)
        rep_all = sb("rep_all", [P, TE4], I32)
        nat = sb("nat", [P, 6, P])
        nat_i = sb("nat_i", [P, 2, P], I32)
        bad = sb("bad", [P, 4])
        general = sb("general", [P, 1])
        general_i = sb("general_i", [P, 1], I32)
        iota_nat = sb("iota_nat", [P, P], I32)
        iota_col = sb("iota_col", [P, TE4], I32)
        half_neg = sb("half_neg", [P, SUB])
        dst_f = sb("dst_f", [P, TE4])
        from_f = sb("from_f", [P, TE4])
        trash = sb("trash", [P, 1])
        e_key = sb("e_key", [P, 2])
        e_cnt = sb("e_cnt", [P, 3])
        e_from = [sb(f"e_from{q}", [P, 1], I32) for q in range(4)]
        e_dst = [sb(f"e_dst{q}", [P, 1], I32) for q in range(4)]
        e_rep = [sb(f"e_rep{q}", [P, 1], I32) for q in range(4)]
        e_row = sb("e_row", [P, 4, P])
        e_eq = sb("e_eq", [P, 2, 3, P], F32R)
        e_junk = sb("e_junk", [P, P])
        e_x = sb("e_x", [P, 2, D])
        e_h = sb("e_h", [P, 2, D])
        e_h_hi = sb("e_h_hi", [P, 2, D], F32R)
        e_h_lo = sb("e_h_lo", [P, 2, D], F32R)
        e_sum = sb("e_sum", [P, 2, D])
        e_bn = sb("e_bn", [P, 6])
        e_mv = sb("e_mv", [P, 2, 3])
        e_rstd = sb("e_rstd", [P, 2, 2])
        g_in = [a1[:, r, :] for r in range(4)]
        g_hi = [a1_hi[:, r, :] for r in range(4)]
        g_lo = [a1_lo[:, r, :] for r in range(4)]
        f_z = [z_out[:, 0, r * H:(r + 1) * H] for r in range(4)]
        f_x = [x_in[:, 0, r * D:(r + 1) * D] for r in range(4)]
        f_sum = [pre2[:, q, :] for q in range(2)]
        f_pre = [ex2[:, q, :] for q in range(2)]
        f_hi = [h2_hi[:, q, :] for q in range(2)]
        f_lo = [h2_lo[:, q, :] for q in range(2)]
        f_res = [h0[:, 0, q * D:(q + 1) * D] for q in range(2)]
        f_out = [x_res[:, 0, q * D:(q + 1) * D] for q in range(2)]
        c_tot = z_b3[:, 0:H]
        w_raw = {1: z_out[:, 0, 0:H], 2: a1[:, :, :].rearrange("p k n -> p (k n)"), 3: z_b3[:, :],
                 4: z_out[:, 1, 0:KC * D]}

        banks = [ctx.enter_context(nc.psum_tensor(f"bank{i}", [P, 512], F32)) for i in range(8)]
        X, Y, HB, OB = banks[0:4], banks[4:6], banks[6], banks[7]

        edges_loaded, consts_loaded, w_loaded = sem("edges_loaded"), sem("consts_loaded"), sem("w_loaded")
        biases_loaded, bias_tr, b_cols_ready = sem("biases_loaded"), sem("bias_tr"), sem("b_cols_ready")
        pool_const = sem("pool_const")
        w_split, w_low = sem("w_split"), sem("w_low")
        setup = sem("setup")
        edge_tr, rows_stored, shifted = sem("edge_tr"), sem("rows_stored"), sem("shifted")
        bad_ready, bad_sum = sem("bad_ready"), sem("bad_sum")
        window_ready, setup_done, agg_zeroed = sem("window_ready"), sem("setup_done"), sem("agg_zeroed")
        row_loaded = [sem(f"row_loaded{q}") for q in range(2)]
        e_idx, e_link, e_compared = sem("e_idx"), sem("e_link"), sem("e_compared")
        gathered = [sem(f"gathered{q}") for q in range(2)]
        e_stat, e_var, e_root, e_nmr = sem("e_stat"), sem("e_var"), sem("e_root"), sem("e_nmr")
        e_h_ready, e_hi_ready, e_lo_ready = sem("e_h_ready"), sem("e_hi_ready"), sem("e_lo_ready")
        e_summed, e_sum_ready = sem("e_summed"), sem("e_sum_ready")
        scattered = [sem(f"scattered{q}") for q in range(2)]
        x_loaded = [sem(f"x_loaded{q}") for q in range(2)]
        agg_loaded = [sem(f"agg_loaded{q}") for q in range(2)]
        res_loaded = [sem(f"res_loaded{q}") for q in range(2)]
        z_stored = [sem(f"z_stored{q}") for q in range(2)]
        out_stored = [sem(f"out_stored{q}") for q in range(2)]
        n_stat, var_ready, root_ready, nmr_ready = sem("n_stat"), sem("var_ready"), sem("root_ready"), sem("nmr_ready")
        h0_ready, h1_ready = sem("h0_ready"), sem("h1_ready")
        hT_ps, hT_hi_ready, hT_lo_ready = sem("hT_ps"), sem("hT_hi_ready"), sem("hT_lo_ready")
        l1_ps, a1_ready, a1_hi_ready, a1_lo_ready = sem("l1_ps"), sem("a1_ready"), sem("a1_hi_ready"), sem("a1_lo_ready")
        l2_ps, pre2_ready, min2_ready, ex2_ready = sem("l2_ps"), sem("pre2_ready"), sem("min2_ready"), sem("ex2_ready")
        h2_ready, h2_hi_ready, h2_lo_ready = sem("h2_ready"), sem("h2_hi_ready"), sem("h2_lo_ready")
        z_ps, z_copied, z_b3_ready = sem("z_ps"), sem("z_copied"), sem("z_b3_ready")
        zT_ps, a3_hi_ready, a3_lo_ready = sem("zT_ps"), sem("a3_hi_ready"), sem("a3_lo_ready")
        l4_ps, oT_ready, o_ps, out_ready = sem("l4_ps"), sem("oT_ready"), sem("o_ps"), sem("out_ready")
        waited = sem("waited")
        c_zeroed = sem("c_zeroed")
        c_idx, c_row, c_gathered, c_done = sem("c_idx"), sem("c_row"), sem("c_gathered"), sem("c_done")
        c_link, c_eq, c_hi, c_lo, c_ps, c_sum = (sem("c_link"), sem("c_eq"), sem("c_hi"), sem("c_lo"), sem("c_ps"),
                                                 sem("c_sum"))
        t_idx, t_xidx, t_ridx = sem("t_idx"), sem("t_xidx"), sem("t_ridx")
        t_row = [sem(f"t_row{r}") for r in range(4)]
        t_g = [sem(f"t_g{r}") for r in range(4)]
        t_z = [sem(f"t_z{r}") for r in range(4)]
        t_x = [sem(f"t_x{r}") for r in range(4)]
        t_stored = [sem(f"t_stored{r}") for r in range(2)]
        t_hi, t_lo, t_eq, t_sum_ps = sem("t_hi"), sem("t_lo"), sem("t_eq"), sem("t_sum_ps")
        t_sum, t_pre, t_tr_ps, t_a_hi, t_a_lo = sem("t_sum"), sem("t_pre"), sem("t_tr_ps"), sem("t_a_hi"), sem("t_a_lo")
        t_o_ps, t_res, t_out = sem("t_o_ps"), sem("t_res"), sem("t_out")

        block = ctx.enter_context(nc.Block())

        def apart(engine):
            engine.sem_inc(waited, 1)

        def node_rows(table, n):
            base = N - ROWS if isinstance(n, int) and n == T - 1 else n * ROWS
            return table[bass.ds(base, ROWS), :].rearrange("(p j) f -> p (j f)", j=SUB)

        def filled(n, q):
            return 8 * (n - q) + 16

        def pair_loop(engine, body, first, last, count):
            stop = first + (count - first - last) // 2 * 2
            for i in range(first):
                body(i, i % 2)
            with engine.Fori(first, stop, 2) as i:
                body(i, 0)
                body(i + 1, 1)
            for i in range(stop, count):
                body(i, i % 2)

        def node_loop(engine, body):
            assert 2 + (T + 1 - 8) // 2 * 2 + E0 <= TE2 <= T + E0 - 3
            pair_loop(engine, body, 2, 6, T + 1)

        def exists(n):
            return not isinstance(n, int) or 0 <= n < T

        def edges_ahead(engine, first, rest):
            for o in range(E0 + 1):
                if o < E0:
                    first(o, o % 2)
                if o > 0:
                    rest(o - 1, (o - 1) % 2)
            general_case = is_general(engine)
            with engine.If(general_case > 0):
                with engine.Fori(E0, TE2, 2) as o:
                    for q in range(2):
                        first(o + q, q)
                        rest(o + q, q)
                engine.wait_ge(e_sum_ready, TE2)
            return general_case

        def edge_part(engine, general_case, part, o, q):
            if o_exists(o):
                with engine.If(general_case < 1):
                    part(o, q)

        def nothing(o, q):
            pass

        def o_exists(o):
            return not isinstance(o, int) or 0 <= o < TE2

        def t_exists(e):
            return not isinstance(e, int) or 0 <= e < TE4

        def filled4(n, r):
            return 4 * (n - r) + 16

        def quad_loop(engine, body):
            stop = 8 + (TE4 - 14) // 4 * 4
            for s in range(-2, 8):
                body(s, s % 4)
            with engine.Fori(8, stop, 4) as s:
                for r in range(4):
                    body(s + r, r)
            for s in range(stop, TE4 + 4):
                body(s, s % 4)

        def is_general(engine):
            engine.wait_ge(setup_done, 1)
            return engine.value_load(general_i[0:1, 0:1], min_val=0, max_val=1)

        def each_tile(engine, body):
            body(0)
            with engine.Fori(1, TE2) as o:
                body(o)

        CHAIN_END = 16 * TE2

        def tail_sync(sp):
            general_case = is_general(sp)
            with sp.If(general_case > 0):
                sp.dma_start(z_sums.rearrange("(p r) f -> p r f", p=P),
                             zeros[:, None, 0:H].broadcast_to([P, SUM_ROWS // P, H])).then_inc(c_zeroed, 16)

                def key_load(o):
                    sp.wait_ge(c_idx, o + 1)
                    sp.dma_start(e_row[:, 0, :], key_rows[None, bass.ds(o * P, P)].broadcast_to([P, P]))\
                      .then_inc(c_row, 16)

                each_tile(sp, key_load)
                sp.wait_ge(c_done, CHAIN_END)
            sp.wait_ge(rows_stored, 32)

            def step(s, r):
                if t_exists(s):
                    wait(sp, t_eq, s - 3)
                    sp.dma_start(e_row[:, r, :], win_rows[None, bass.ds(s * P, P)].broadcast_to([P, P]))\
                      .then_inc(t_row[r], 16)

            quad_loop(sp, step)

        def tail_pool(pool):
            for n in (T - 2, T - 1):
                pool.wait_ge(out_stored[n % 2], filled(n, n % 2))
                pool.wait_ge(z_stored[n % 2], filled(n, n % 2))
            def step(s, r, summed):
                r2 = (r + 2) % 4
                if t_exists(s + 2):
                    pool.wait_ge(t_idx, 2 * (s + 3))
                    wait(pool, t_lo, s - 1)
                    apart(pool)
                    pool.indirect_dma_start(g_in[r2], None, summed,
                                            bass.IndirectOffsetOnAxis(ap=e_from[r2][:, 0:1], axis=0))\
                        .then_inc(t_g[r2], 16)
                    wait(pool, t_sum, s - 1)
                    apart(pool)
                    pool.indirect_dma_start(f_z[r2], None, z_table,
                                            bass.IndirectOffsetOnAxis(ap=e_dst[r2][:, 0:1], axis=0))\
                        .then_inc(t_z[r2], 16)
                if t_exists(s):
                    wait(pool, t_res, s - 3)
                    apart(pool)
                    pool.indirect_dma_start(f_x[r], None, x,
                                            bass.IndirectOffsetOnAxis(ap=e_dst[r][:, 0:1], axis=0))\
                        .then_inc(t_x[r], 16)
                e, q = s - 4, r % 2
                if t_exists(e):
                    pool.wait_ge(t_out, 2 * (e + 1))
                    if not isinstance(e, int) or e > 0:
                        pool.wait_ge(t_stored[1 - q], filled(e - 1, 1 - q))
                    apart(pool)
                    pool.indirect_dma_start(out, bass.IndirectOffsetOnAxis(ap=e_rep[q][:, 0:1], axis=0),
                                            f_out[q], None, bounds_check=N - 1, oob_is_err=False)\
                        .then_inc(t_stored[q], 16)

            general_case = is_general(pool)
            with pool.If(general_case > 0):
                def add(o):
                    pool.wait_ge(c_idx, o + 1)
                    apart(pool)
                    pool.indirect_dma_start(g_in[0], None, z_table,
                                            bass.IndirectOffsetOnAxis(ap=e_from[0][:, 0:1], axis=0))\
                        .then_inc(c_gathered, 16)
                    pool.wait_ge(c_sum, o + 1)
                    apart(pool)
                    pool.indirect_dma_start(z_sums, bass.IndirectOffsetOnAxis(ap=e_rep[0][:, 0:1], axis=0),
                                            c_tot, None, compute_op=ALU.add).then_inc(c_done, 16)

                pool.wait_ge(c_zeroed, 16)
                each_tile(pool, add)
                pool.wait_ge(c_done, CHAIN_END)
                quad_loop(pool, lambda s, r: step(s, r, z_sums))
            with pool.Else():
                quad_loop(pool, lambda s, r: step(s, r, z_table))
            for e in (TE4 - 2, TE4 - 1):
                pool.wait_ge(t_stored[e % 2], filled(e, e % 2))

        def tail_act(act):
            general_case = is_general(act)
            with act.If(general_case > 0):
                def add(o):
                    act.wait_ge(c_gathered, 16 * (o + 1))
                    act.activation(g_hi[0], g_in[0], ACT.Copy).then_inc(c_hi, 1)
                    act.wait_ge(c_ps, o + 1)
                    act.activation(c_tot, Y[0][:, :], ACT.Copy).then_inc(c_sum, 1)

                each_tile(act, add)

            def step(s, r):
                if t_exists(s):
                    act.wait_ge(t_g[r], filled4(s, r))
                    wait(act, t_sum_ps, s - 2)
                    act.activation(g_hi[r], g_in[r], ACT.Copy).then_inc(t_hi, 1)
                e, q = s - 2, r % 2
                if t_exists(e):
                    act.wait_ge(t_tr_ps, e + 1)
                    wait(act, t_o_ps, e - 1)
                    act.activation(f_hi[q], X[q][:, :], ACT.Relu).then_inc(t_a_hi, 1)

            quad_loop(act, step)

        def tail_dve(dve):
            general_case = is_general(dve)
            with dve.If(general_case > 0):
                def add(o):
                    wait(dve, c_done, 16 * o)
                    dve.tensor_copy(e_from[0][:, :], src_all[:, bass.ds(o, 1)]).then_inc(c_link, 1)
                    dve.tensor_copy(e_key[:, 0:1], key_all[:, bass.ds(o, 1)]).then_inc(c_link, 1)
                    dve.wait_ge(c_link, 2 * (o + 1))
                    dve.tensor_copy(e_rep[0][:, :], rep_all[:, bass.ds(o, 1)]).then_inc(c_idx, 1)
                    dve.wait_ge(c_row, 16 * (o + 1))
                    dve.tensor_scalar(e_eq[:, 0, 0, :], e_row[:, 0, :], e_key[:, 0:1], None, ALU.is_equal)\
                       .then_inc(c_eq, 1)
                    dve.wait_ge(c_hi, o + 1)
                    dve.tensor_tensor(g_lo[0], g_in[0], g_hi[0].bitcast(F32), ALU.subtract).then_inc(c_lo, 1)

                each_tile(dve, add)
                dve.wait_ge(c_done, CHAIN_END)

            def step(s, r):
                r2, r1, q = (r + 2) % 4, (r + 3) % 4, r % 2
                if t_exists(s + 2):
                    for done in (t_g, t_z, t_x):
                        wait(dve, done[r2], filled4(s + 2, r2) - 16)
                    dve.tensor_copy(e_from[r2][:, :], from_all[:, bass.ds(s + 2, 1)]).then_inc(t_idx, 1)
                    dve.tensor_copy(e_dst[r2][:, :], dst_all[:, bass.ds(s + 2, 1)]).then_inc(t_idx, 1)
                e = s - 1
                if t_exists(e):
                    dve.wait_ge(t_row[r1], filled4(e, r1))
                    wait(dve, t_sum_ps, e - 1)
                    for d in (-1, 0, 1):
                        if t_exists(e + d):
                            last = dve.tensor_scalar(e_eq[:, 1 - q, d + 1, :], e_row[:, r1, :],
                                                     win_all[:, bass.ds(e + d, 1)], None, ALU.is_equal)
                    last.then_inc(t_eq, 1)
                if t_exists(s):
                    dve.wait_ge(t_hi, s + 1)
                    wait(dve, t_sum_ps, s - 2)
                    dve.tensor_tensor(g_lo[r], g_in[r], g_hi[r].bitcast(F32), ALU.subtract).then_inc(t_lo, 1)
                e = s - 2
                if t_exists(e):
                    dve.wait_ge(t_a_hi, e + 1)
                    wait(dve, t_o_ps, e - 1)
                    dve.scalar_tensor_tensor(f_lo[q], X[q][:, :], 0.0, f_hi[q].bitcast(F32), ALU.max, ALU.subtract)\
                       .then_inc(t_a_lo, 1)
                e = s - 3
                if t_exists(e):
                    dve.wait_ge(t_o_ps, e + 1)
                    dve.wait_ge(t_x[(r + 1) % 4], filled4(e, (r + 1) % 4))
                    dve.tensor_tensor(f_res[1 - q], X[3 - q][:, 0:D], f_x[(r + 1) % 4], ALU.add).then_inc(t_res, 1)
                    wait(dve, t_stored[1 - q], filled(e, 1 - q) - 16)
                    dve.tensor_copy(e_rep[1 - q][:, :], rep_all[:, bass.ds(e, 1)]).then_inc(t_out, 1)
                    dve.wait_ge(t_res, e + 1)
                    dve.tensor_tensor(f_out[1 - q], f_res[1 - q], b4_row[:, :], ALU.add).then_inc(t_out, 1)
                e = s - 1
                if t_exists(e):
                    dve.wait_ge(t_sum_ps, e + 1)
                    dve.wait_ge(t_z[r1], filled4(e, r1))
                    dve.tensor_tensor(f_sum[1 - q], Y[1 - q][:, :], f_z[r1], ALU.add).then_inc(t_sum, 1)
                    dve.wait_ge(t_sum, e + 1)
                    wait(dve, t_tr_ps, e - 1)
                    dve.tensor_tensor(f_pre[1 - q], f_sum[1 - q], b3_row[:, :], ALU.add).then_inc(t_pre, 1)

            quad_loop(dve, step)

        def tail_pe(pe, product):
            general_case = is_general(pe)
            with pe.If(general_case > 0):
                def add(o):
                    pe.wait_ge(c_eq, o + 1)
                    pe.wait_ge(c_lo, o + 1)
                    pe.matmul(Y[0][:, :], e_eq[:, 0, 0, :], g_hi[0], start=True, stop=False)
                    pe.matmul(Y[0][:, :], e_eq[:, 0, 0, :], g_lo[0], start=False, stop=True).then_inc(c_ps, 1)

                each_tile(pe, add)

            def step(s, r):
                q = r % 2
                e = s - 2
                if t_exists(e):
                    pe.wait_ge(t_pre, e + 1)
                    wait(pe, t_a_lo, e - 1)
                    for c in range(KC):
                        last = pe.transpose(X[q][:, c * P:(c + 1) * P], f_pre[q][:, c * P:(c + 1) * P], ident[:, :])
                    last.then_inc(t_tr_ps, 1)
                e = s - 3
                if t_exists(e):
                    pe.wait_ge(t_a_lo, e + 1)
                    wait(pe, t_res, e - 1)
                    product(X[3 - q][:, 0:D], lambda a, k: (f_hi, f_lo)[a][1 - q][:, k * P:(k + 1) * P],
                            lambda b, k: (w_hi, w_lo)[b][4][:, k * D:(k + 1) * D], KC).then_inc(t_o_ps, 1)
                e = s - 1
                if t_exists(e):
                    pe.wait_ge(t_lo, s + 1 if t_exists(s) else TE4)
                    pe.wait_ge(t_eq, e + 1)
                    wait(pe, t_sum, e - 1)
                    blocks = [d for d in (-1, 0, 1) if t_exists(e + d)]
                    for d in blocks:
                        for m, part in enumerate((g_hi, g_lo)):
                            last = pe.matmul(Y[1 - q][:, :], e_eq[:, 1 - q, d + 1, :], part[(r + 3 + d) % 4],
                                             start=(d == blocks[0] and m == 0), stop=(d == blocks[-1] and m == 1))
                    last.then_inc(t_sum_ps, 1)

            quad_loop(pe, step)


        @block.sync
        def _(sp):
            sp.wait_ge(pool_const, 2)
            for k, table in enumerate((dst, src)):
                sp.dma_start(nat_i[0:TE - 1, k, :], table[0:(TE - 1) * P].rearrange("(t c) -> t c", c=P))\
                  .then_inc(edges_loaded, 16)
                sp.dma_start(nat_i[TE - 1:TE, k, 0:LAST_E], table[(TE - 1) * P:E].rearrange("(t c) -> t c", t=1))\
                  .then_inc(edges_loaded, 16)
            sp.dma_start(z_out[:, 0, 0:H], w1).then_inc(w_loaded, 16)
            sp.dma_start(a1[:, :, :], w2.rearrange("(k p) n -> p k n", p=P)).then_inc(w_loaded, 16)
            sp.dma_start(z_b3[:, :].rearrange("p (k n) -> p k n", k=KC), w3.rearrange("(k p) n -> p k n", p=P))\
              .then_inc(w_loaded, 16)
            sp.dma_start(z_out[:, 1, 0:KC * D].rearrange("p (k n) -> p k n", k=KC),
                         w4.rearrange("(k p) n -> p k n", p=P)).then_inc(w_loaded, 16)
            sp.wait_ge(pool_const, 3)
            sp.dma_start(agg_table.rearrange("(p r) f -> p r f", p=P),
                         zeros[:, None, 0:D].broadcast_to([P, SUM_ROWS // P, D])).then_inc(agg_zeroed, 16)
            sp.wait_ge(setup, 2)
            sp.dma_start(key_rows.rearrange("(t c) -> t c", c=P), nat[0:TE4, 0, :]).then_inc(rows_stored, 16)
            sp.wait_ge(rows_stored, 16)
            span = (TE4 - 2) * P
            sp.dma_start(nat[0:TE4 - 2, 2, :], key_rows[1:1 + span].rearrange("(t c) -> t c", c=P)).then_inc(shifted, 16)
            sp.dma_start(nat[0:TE4 - 2, 3, :], key_rows[P + 1:P + 1 + span].rearrange("(t c) -> t c", c=P))\
              .then_inc(shifted, 16)

            def edge_load(o, q):
                wait(sp, e_compared, o - 1)
                sp.dma_start(e_row[:, q, :], key_rows[None, bass.ds(o * P, P)].broadcast_to([P, P]))\
                  .then_inc(row_loaded[q], 16)

            general_case = edges_ahead(sp, edge_load, nothing)
            sp.wait_ge(window_ready, 1)
            sp.dma_start(win_rows.rearrange("(t c) -> t c", c=P), nat[0:TE4, 4, :]).then_inc(rows_stored, 16)

            def load_x(n, q):
                wait(sp, h0_ready, n - 1)
                sp.dma_start(x_in[:, q, :], node_rows(x, n)).then_inc(x_loaded[q], 16)

            def load_agg(n, q):
                wait(sp, hT_ps, n - 1)
                o = min(n + E0 - 4, TE2 - 1) if isinstance(n, int) else n + E0 - 4
                odd = o % 2 if isinstance(n, int) else q
                sp.wait_ge(scattered[odd], filled(o, odd))
                sp.dma_start(agg_in[:, q, :], node_rows(agg_table, n)).then_inc(agg_loaded[q], 16)

            def step(i, q):
                if isinstance(i, int) and i == 0:
                    sp.wait_ge(w_low, 4)
                    for n in range(3):
                        load_x(n, n % 2)
                        load_agg(n, n % 2) if n < 2 else None
                edge_part(sp, general_case, edge_load, i + E0, q)
                if exists(i + 3):
                    load_x(i + 3, 1 - q)
                if exists(i + 2):
                    load_agg(i + 2, q)
                if exists(i):
                    wait(sp, out_stored[q], filled(i, q) - 16)
                    sp.dma_start(x_res[:, q, :], node_rows(x, i)).then_inc(res_loaded[q], 16)
                if exists(i - 1):
                    sp.wait_ge(out_ready, i)
                    if isinstance(i, int) and i == T:
                        sp.wait_ge(out_stored[q], filled(T - 2, q))
                    sp.dma_start(node_rows(out, i - 1), x_res[:, 1 - q, :]).then_inc(out_stored[1 - q], 16)
                if exists(i):
                    sp.wait_ge(z_copied, SUB * (i + 1))
                    if isinstance(i, int) and i == T - 1:
                        sp.wait_ge(z_stored[1 - q], filled(T - 2, 1 - q))
                    sp.dma_start(node_rows(z_table, i), z_out[:, q, :]).then_inc(z_stored[q], 16)

            node_loop(sp, step)
            tail_sync(sp)

        @block.gpsimd
        def _(pool):
            pool.iota(nat_i[0:TE4, 0, :], pattern=[[1, P]], base=N - (TE - 1) * P, channel_multiplier=P)\
                .then_inc(pool_const, 1)
            pool.memset(nat_i[0:TE4, 1, :], 0).then_inc(pool_const, 1)
            pool.memset(zeros[:, :], 0.0).then_inc(pool_const, 1)
            pool.memset(ones[:, :], 1.0).then_inc(pool_const, 1)
            pool.memset(ident[:, :], 0.0).then_inc(pool_const, 1)
            pool.wait_ge(pool_const, 5)
            pool.affine_select(out=ident[:, :], in_=ident[:, :], compare_op=ALU.not_equal, fill=1.0, base=0,
                               pattern=[[-1, P]], channel_multiplier=1).then_inc(pool_const, 1)
            pool.affine_select(out=upper[:, :], in_=ones[:, :], compare_op=ALU.is_gt, fill=0.0, base=0,
                               pattern=[[1, P]], channel_multiplier=-1).then_inc(pool_const, 1)
            pool.iota(rep_all[:, :], pattern=[[0, TE4]], base=TRASH, channel_multiplier=1).then_inc(pool_const, 1)
            pool.iota(iota_nat[0:TE4, :], pattern=[[1, P]], base=0, channel_multiplier=P).then_inc(pool_const, 1)
            pool.iota(iota_col[:, :], pattern=[[P, TE4]], base=0, channel_multiplier=1).then_inc(pool_const, 1)
            pool.memset(half_neg[:, :], -0.5).then_inc(pool_const, 1)

            def gather(o, q):
                pool.wait_ge(e_idx, o + 1)
                wait(pool, e_h_ready, o - 1)
                apart(pool)
                pool.indirect_dma_start(e_x[:, q, :], None, x,
                                        bass.IndirectOffsetOnAxis(ap=e_from[q][:, 0:1], axis=0))\
                    .then_inc(gathered[q], 16)

            def inverse_root(o, q):
                pool.wait_ge(e_var, o + 1)
                wait(pool, e_nmr, o - 1)
                pool.tensor_tensor(e_rstd[:, q, 0:1], e_mv[:, q, 2:3], half_neg[:, 0:1], ALU.pow).then_inc(e_root, 1)

            def scatter(o, q):
                pool.wait_ge(e_sum_ready, o + 1)
                pool.wait_ge(e_link, 6 * o + 6)
                if not isinstance(o, int) or o > 0:
                    pool.wait_ge(scattered[1 - q], filled(o - 1, 1 - q))
                apart(pool)
                pool.indirect_dma_start(agg_table, bass.IndirectOffsetOnAxis(ap=e_rep[q][:, 0:1], axis=0),
                                        e_sum[:, q, :], None, compute_op=ALU.add).then_inc(scattered[q], 16)

            pool.wait_ge(agg_zeroed, 16)

            def root_and_scatter(o, q):
                inverse_root(o, q)
                scatter(o, q)

            general_case = edges_ahead(pool, gather, root_and_scatter)

            def step(i, q):
                if isinstance(i, int) and i == 0:
                    for n in range(2):
                        node_root(n, n % 2)
                        node_add(n, n % 2)
                    low_a1(0)
                o = i + E0 - 1
                edges = not isinstance(i, int) or i > 0
                if exists(i + 2):
                    node_root(i + 2, q)
                if edges:
                    edge_part(pool, general_case, inverse_root, o, 1 - q)
                if exists(i):
                    for c in range(KC):
                        g = KC * i + c
                        pool.wait_ge(h2_hi_ready, g + 1)
                        pool.tensor_tensor(h2_lo[:, c, :], h2[:, c % 2, :], h2_hi[:, c, :].bitcast(F32), ALU.subtract)\
                            .then_inc(h2_lo_ready, 1)
                if exists(i + 2):
                    node_add(i + 2, q)
                if exists(i + 1):
                    low_a1(i + 1)
                if edges:
                    edge_part(pool, general_case, scatter, o, 1 - q)
                edge_part(pool, general_case, gather, i + E0, q)

            def node_root(n, q):
                pool.wait_ge(var_ready, n + 1)
                wait(pool, nmr_ready, n - 1)
                pool.tensor_tensor(rstd[:, q, :], mv[:, q, :, 1], half_neg[:, 0:SUB], ALU.pow).then_inc(root_ready, 1)

            def node_add(n, q):
                pool.wait_ge(h0_ready, n + 1)
                pool.wait_ge(agg_loaded[q], filled(n, q))
                pool.tensor_tensor(agg_in[:, q, :], agg_in[:, q, :], h0[:, q, :], ALU.add).then_inc(h1_ready, 1)

            def low_a1(n):
                for c in range(KC):
                    g = KC * n + c
                    pool.wait_ge(a1_ready, g + 1)
                    pool.wait_ge(a1_hi_ready, g + 1)
                    pool.tensor_tensor(a1_lo[:, c, :], a1[:, c, :], a1_hi[:, c, :].bitcast(F32), ALU.subtract)\
                        .then_inc(a1_lo_ready, 1)

            node_loop(pool, step)
            tail_pool(pool)

        @block.scalar
        def _(act):
            for at, table in ((0, b1), (KC, b2), (2 * KC, b4)):
                rows = table.shape[0] // P
                act.dma_start(b_nat[at:at + rows, :], table.rearrange("(c p) -> c p", p=P)).then_inc(biases_loaded, 16)
            act.dma_start(b3_row[:, :], b3[None, :].broadcast_to([P, H])).then_inc(consts_loaded, 16)
            act.dma_start(b4_row[:, :], b4[None, :].broadcast_to([P, D])).then_inc(consts_loaded, 16)
            act.wait_ge(w_loaded, 64)
            for n in range(1, 5):
                act.activation(w_hi[n][:, :], w_raw[n], ACT.Copy).then_inc(w_split, 1)

            def edge_h(o, q):
                act.wait_ge(e_nmr, o + 1)
                wait(act, e_lo_ready, o - 1)
                act.activation(e_h[:, q, :], e_x[:, q, :], ACT.Relu, bias=e_rstd[:, q, 1:2], scale=e_rstd[:, q, 0:1])\
                   .then_inc(e_h_ready, 1)
                act.wait_ge(e_h_ready, o + 1)
                wait(act, e_summed, o - 1)
                act.activation(e_h_hi[:, q, :], e_h[:, q, :], ACT.Copy).then_inc(e_hi_ready, 1)

            def edge_sum(o, q):
                act.wait_ge(e_summed, o + 1)
                wait(act, scattered[q], filled(o, q) - 16)
                act.activation(e_sum[:, q, :], HB[:, 0:D], ACT.Copy).then_inc(e_sum_ready, 1)

            def h_and_sum(o, q):
                edge_h(o, q)
                edge_sum(o, q)

            general_case = edges_ahead(act, nothing, h_and_sum)

            def norm(n, q):
                act.wait_ge(nmr_ready, n + 1)
                wait(act, h1_ready, n - 1)
                for j in range(SUB):
                    last = act.activation(h0[:, q, j * D:(j + 1) * D], x_in[:, q, j * D:(j + 1) * D], ACT.Relu,
                                          bias=nmr[:, q, j:j + 1], scale=rstd[:, q, j:j + 1])
                last.then_inc(h0_ready, 1)

            def upper_hT(n):
                act.wait_ge(hT_ps, n + 1)
                act.activation(hT_hi[:, :], HB[:, :], ACT.Copy).then_inc(hT_hi_ready, 1)

            def relu_a1(n):
                for c in range(KC):
                    act.wait_ge(l1_ps, KC * n + c + 1)
                    act.activation(a1[:, c, :], X[c][:, :], ACT.Relu, bias=b1_col[:, c:c + 1]).then_inc(a1_ready, 1)

            def step(i, q):
                if isinstance(i, int) and i == 0:
                    act.wait_ge(b_cols_ready, 1)
                    norm(0, 0)
                    norm(1, 1)
                    upper_hT(0)
                    relu_a1(0)
                o = i + E0 - 1
                edges = not isinstance(i, int) or i > 0
                if exists(i + 1):
                    upper_hT(i + 1)
                for c in range(KC):
                    g = KC * i + c
                    if exists(i):
                        act.wait_ge(l2_ps, g + 1)
                        wait(act, h2_ready, g - 1)
                        act.activation(pre2[:, c % 2, :], Y[c % 2][:, :], ACT.Identity, bias=b2_col[:, c:c + 1])\
                           .then_inc(pre2_ready, 1)
                        act.wait_ge(min2_ready, g + 1)
                        act.activation(ex2[:, c % 2, :], ex2[:, c % 2, :], ACT.Exp).then_inc(ex2_ready, 1)
                        act.wait_ge(h2_ready, g + 1)
                        act.activation(h2_hi[:, c, :], h2[:, c % 2, :], ACT.Copy).then_inc(h2_hi_ready, 1)
                    if exists(i - 1) and c < KC // 2:
                        for f in (2 * c, 2 * c + 1):
                            act.wait_ge(zT_ps, KC * (i - 1) + f + 1)
                            act.activation(a3_hi[:, f, :], X[f][:, :], ACT.Relu).then_inc(a3_hi_ready, 1)
                    if c == 1 and edges:
                        edge_part(act, general_case, edge_h, o, 1 - q)
                    if c == 2 and exists(i + 2):
                        norm(i + 2, q)
                if exists(i + 1):
                    relu_a1(i + 1)
                if exists(i - 1):
                    act.wait_ge(l4_ps, i)
                    act.activation(oT[:, :], OB[:, :], ACT.Identity, bias=b4_col[:, 0:1]).then_inc(oT_ready, 1)
                if edges:
                    edge_part(act, general_case, edge_sum, o, 1 - q)
                if exists(i):
                    wait(act, z_stored[q], filled(i, q) - 16)
                    for j in range(SUB):
                        act.wait_ge(z_ps, SUB * i + j + 1)
                        act.activation(z_out[:, q, j * H:(j + 1) * H], Y[j % 2][:, :], ACT.Copy).then_inc(z_copied, 1)

            node_loop(act, step)
            tail_act(act)

        @block.vector
        def _(dve):
            chain = [0]

            def link(instruction):
                chain[0] += 1
                instruction.then_inc(setup, 1)
                dve.wait_ge(setup, chain[0])

            dve.wait_ge(edges_loaded, 64)
            link(dve.tensor_copy(nat[0:TE4, 0, :], nat_i[0:TE4, 0, :]))
            link(dve.tensor_copy(nat[0:TE4, 1, :], nat_i[0:TE4, 1, :]))
            dve.wait_ge(pool_const, 11)
            link(dve.tensor_copy(trash[:, :], rep_all[:, 0:1]))
            dve.wait_ge(edge_tr, 2)
            link(dve.tensor_copy(key_all[:, :], X[0][:, 0:TE4]))
            link(dve.tensor_copy(src_f[:, :], X[1][:, 0:TE4]))
            link(dve.tensor_copy(src_all[:, :], src_f[:, :]))
            dve.wait_ge(bias_tr, 1)
            dve.tensor_copy(b_cols[:, :], X[3][:, 0:NB]).then_inc(b_cols_ready, 1)
            for n in range(1, 5):
                dve.wait_ge(w_split, n)
                dve.tensor_tensor(w_lo[n][:, :], w_raw[n], w_hi[n][:, :].bitcast(F32), ALU.subtract)\
                   .then_inc(w_low, 1)
            dve.wait_ge(shifted, 32)
            R = TE4 - 2
            link(dve.tensor_tensor(nat[0:R, 2, :], nat[0:R, 0, :], nat[0:R, 2, :], ALU.is_gt))
            link(dve.tensor_tensor(nat[0:R, 3, :], nat[0:R, 0, :], nat[0:R, 3, :], ALU.is_ge))
            link(dve.tensor_tensor(nat[0:R, 2, :], nat[0:R, 2, :], nat[0:R, 3, :], ALU.add))
            link(dve.tensor_copy(bad[:, 2:3], iota_col[:, 0:1]))
            link(dve.tensor_scalar(bad[:, 2:3], bad[:, 2:3], float(ROWS), float((4 - E0) * ROWS), ALU.mult, ALU.add))
            link(dve.tensor_tensor(bad[0:R, 3:4], bad[0:R, 2:3], nat[0:R, 0, 0:1], ALU.is_gt))
            link(dve.tensor_tensor(nat[0:R, 2, 0:1], nat[0:R, 2, 0:1], bad[0:R, 3:4], ALU.add))
            dve.reduce_sum(bad[0:R, 0:1], nat[0:R, 2, :], axis=mybir.AxisListType.X).then_inc(bad_ready, 1)
            dve.wait_ge(bad_sum, 1)
            link(dve.tensor_scalar(general[:, :], X[2][:, 0:1], 1.0, None, ALU.min))
            dve.tensor_copy(general_i[:, :], general[:, :]).then_inc(setup_done, 1)
            link(dve.tensor_copy(nat[0:TE4, 5, :], iota_nat[0:TE4, :]))
            link(dve.tensor_tensor(nat[0:TE4, 5, :], nat[0:TE4, 5, :], nat[0:TE4, 0, :], ALU.subtract))
            link(dve.scalar_tensor_tensor(nat[0:TE4, 4, :], nat[0:TE4, 5, :], general[0:TE4, 0:1], nat[0:TE4, 0, :],
                                          ALU.mult, ALU.add))
            dve.tensor_copy(bad[:, 1:2], general[:, :]).then_inc(window_ready, 1)
            link(dve.tensor_copy(win_all[:, :], iota_col[:, :]))
            link(dve.tensor_tensor(win_all[:, :], win_all[:, :], key_all[:, :], ALU.subtract))
            link(dve.scalar_tensor_tensor(win_all[:, :], win_all[:, :], general[:, 0:1], key_all[:, :],
                                          ALU.mult, ALU.add))
            link(dve.scalar_tensor_tensor(dst_f[:, :], key_all[:, :], float(N), key_all[:, :], ALU.is_lt, ALU.mult))
            link(dve.tensor_copy(dst_all[:, :], dst_f[:, :]))
            link(dve.tensor_tensor(from_f[:, :], dst_f[:, :], src_f[:, :], ALU.subtract))
            link(dve.scalar_tensor_tensor(from_all[:, :], from_f[:, :], general[:, 0:1], src_f[:, :],
                                          ALU.mult, ALU.add))

            def edge_index(o, q):
                wait(dve, gathered[q], filled(o, q) - 16)
                dve.tensor_copy(e_from[q][:, :], src_all[:, bass.ds(o, 1)]).then_inc(e_idx, 1)
                dve.tensor_copy(e_key[:, q:q + 1], key_all[:, bass.ds(o, 1)]).then_inc(e_link, 1)
                dve.wait_ge(e_link, 6 * o + 1)
                dve.wait_ge(row_loaded[q], filled(o, q))
                wait(dve, e_summed, o - 1)
                dve.tensor_scalar(e_eq[:, q, 0, :], e_row[:, q, :], e_key[:, q:q + 1], None, ALU.is_equal)\
                   .then_inc(e_link, 1)
                dve.scalar_tensor_tensor(e_junk[:, :], e_row[:, q, :], e_key[:, q:q + 1], upper[:, :],
                                         ALU.is_equal, ALU.mult, accum_out=e_cnt[:, 0:1]).then_inc(e_compared, 1)
                dve.tensor_tensor(e_cnt[:, 1:2], trash[:, :], e_key[:, q:q + 1], ALU.subtract).then_inc(e_link, 1)
                dve.wait_ge(e_link, 6 * o + 3)
                dve.wait_ge(e_compared, o + 1)
                dve.scalar_tensor_tensor(e_cnt[:, 2:3], e_cnt[:, 0:1], 1.0, e_cnt[:, 1:2], ALU.min, ALU.mult)\
                   .then_inc(e_link, 1)
                dve.wait_ge(e_link, 6 * o + 4)
                wait(dve, scattered[q], filled(o, q) - 16)
                dve.tensor_tensor(e_rep[q][:, :], e_cnt[:, 2:3], e_key[:, q:q + 1], ALU.add).then_inc(e_link, 1)
                dve.wait_ge(e_link, 6 * o + 5)
                dve.tensor_copy(rep_all[:, bass.ds(o, 1)], e_rep[q][:, :]).then_inc(e_link, 1)

            def edge_stats(o, q):
                dve.wait_ge(gathered[q], filled(o, q))
                dve.bn_stats(e_bn[:, :], e_x[:, q, :]).then_inc(e_stat, 1)
                dve.wait_ge(e_stat, 2 * o + 1)
                wait(dve, e_root, o - 1)
                apart(dve)
                dve.bn_aggr(e_mv[:, q, 0:2], e_bn[:, :]).then_inc(e_stat, 1)
                dve.wait_ge(e_stat, 2 * o + 2)
                dve.tensor_scalar(e_mv[:, q, 2:3], e_mv[:, q, 1:2], EPS, None, ALU.add).then_inc(e_var, 1)

            def edge_bias(o, q):
                dve.wait_ge(e_root, o + 1)
                wait(dve, e_h_ready, o - 1)
                dve.scalar_tensor_tensor(e_rstd[:, q, 1:2], e_mv[:, q, 0:1], -1.0, e_rstd[:, q, 0:1],
                                         ALU.mult, ALU.mult).then_inc(e_nmr, 1)

            def edge_low(o, q):
                dve.wait_ge(e_hi_ready, o + 1)
                wait(dve, e_summed, o - 1)
                dve.tensor_tensor(e_h_lo[:, q, :], e_h[:, q, :], e_h_hi[:, q, :].bitcast(F32), ALU.subtract)\
                   .then_inc(e_lo_ready, 1)

            def edge_norm(o, q):
                edge_stats(o, q)
                edge_bias(o, q)
                edge_low(o, q)

            general_case = edges_ahead(dve, edge_index, edge_norm)

            def norm(n, q):
                dve.wait_ge(x_loaded[q], filled(n, q))
                for j in range(SUB):
                    last = dve.bn_stats(bn[:, j, :], x_in[:, q, j * D:(j + 1) * D])
                last.then_inc(n_stat, 1)
                dve.wait_ge(n_stat, 2 * n + 1)
                wait(dve, nmr_ready, n - 1)
                apart(dve)
                for j in range(SUB):
                    last = dve.bn_aggr(mv[:, q, j, :], bn[:, j, :])
                last.then_inc(n_stat, 1)
                dve.wait_ge(n_stat, 2 * n + 2)
                wait(dve, root_ready, n - 1)
                dve.tensor_scalar(mv[:, q, :, 1], mv[:, q, :, 1], EPS, None, ALU.add).then_inc(var_ready, 1)

            def norm_bias(n, q):
                dve.wait_ge(root_ready, n + 1)
                wait(dve, h0_ready, n - 1)
                dve.scalar_tensor_tensor(nmr[:, q, :], mv[:, q, :, 0], -1.0, rstd[:, q, :], ALU.mult, ALU.mult)\
                   .then_inc(nmr_ready, 1)

            def low_hT(n):
                dve.wait_ge(hT_hi_ready, n + 1)
                dve.tensor_tensor(hT_lo[:, :], HB[:, :], hT_hi[:, :].bitcast(F32), ALU.subtract)\
                   .then_inc(hT_lo_ready, 1)

            def upper_a1(n):
                for c in range(KC):
                    dve.wait_ge(a1_ready, KC * n + c + 1)
                    dve.tensor_copy(a1_hi[:, c, :], a1[:, c, :]).then_inc(a1_hi_ready, 1)

            def step(i, q):
                if isinstance(i, int) and i == 0:
                    dve.wait_ge(consts_loaded, 32)
                    dve.wait_ge(b_cols_ready, 1)
                    for n in range(2):
                        norm(n, n)
                        norm_bias(n, n)
                    low_hT(0)
                    upper_a1(0)
                if exists(i + 1):
                    low_hT(i + 1)
                if exists(i + 2):
                    norm(i + 2, q)
                o = i + E0 - 1
                edges = not isinstance(i, int) or i > 0
                if edges:
                    edge_part(dve, general_case, edge_stats, o, 1 - q)
                for c in range(KC):
                    if c == 1 and edges:
                        edge_part(dve, general_case, edge_bias, o, 1 - q)
                    if c == 3 and edges:
                        edge_part(dve, general_case, edge_low, o, 1 - q)
                    g = KC * i + c
                    if exists(i):
                        dve.wait_ge(pre2_ready, g + 1)
                        wait(dve, h2_ready, g - 1)
                        dve.tensor_scalar(ex2[:, c % 2, :], pre2[:, c % 2, :], 0.0, None, ALU.min)\
                           .then_inc(min2_ready, 1)
                    if c == 0 and exists(i + 2):
                        norm_bias(i + 2, q)
                    if exists(i):
                        dve.wait_ge(ex2_ready, g + 1)
                        wait(dve, h2_lo_ready, g - 1)
                        dve.scalar_tensor_tensor(h2[:, c % 2, :], ex2[:, c % 2, :], -1.0, pre2[:, c % 2, :],
                                                 ALU.add, ALU.max).then_inc(h2_ready, 1)
                    if exists(i - 1) and c < KC // 2:
                        for f in (2 * c, 2 * c + 1):
                            dve.wait_ge(a3_hi_ready, KC * (i - 1) + f + 1)
                            dve.scalar_tensor_tensor(a3_lo[:, f, :], X[f][:, :], 0.0, a3_hi[:, f, :].bitcast(F32),
                                                     ALU.max, ALU.subtract).then_inc(a3_lo_ready, 1)
                if exists(i + 1):
                    upper_a1(i + 1)
                edge_part(dve, general_case, edge_index, i + E0, q)

                def z_add(j):
                    dve.wait_ge(z_copied, SUB * i + j + 1)
                    dve.tensor_tensor(z_b3[:, j * H:(j + 1) * H], z_out[:, q, j * H:(j + 1) * H], b3_row[:, :], ALU.add)\
                       .then_inc(z_b3_ready, 1)

                if exists(i):
                    z_add(0)
                    z_add(1)
                if exists(i - 1):
                    dve.wait_ge(o_ps, i)
                    dve.wait_ge(res_loaded[1 - q], filled(i - 1, 1 - q))
                    dve.tensor_tensor(x_res[:, 1 - q, :], x_res[:, 1 - q, :], HB[:, :], ALU.add).then_inc(out_ready, 1)
                if exists(i):
                    z_add(2)
                    z_add(3)

            node_loop(dve, step)
            tail_dve(dve)

        @block.tensor
        def _(pe):
            def product(ps, left, right, ks):
                for k in range(ks):
                    parts = ((0, 0), (0, 1), (1, 0))
                    for m, (a, b) in enumerate(parts):
                        last = pe.matmul(ps, left(a, k), right(b, k), start=(k == 0 and m == 0),
                                         stop=(k == ks - 1 and m == 2))
                return last

            W = {n: (w_hi[n], w_lo[n]) for n in range(1, 5)}
            HT, A1, H2, A3 = (hT_hi, hT_lo), (a1_hi, a1_lo), (h2_hi, h2_lo), (a3_hi, a3_lo)

            pe.wait_ge(pool_const, 6)
            pe.wait_ge(setup, 2)
            pe.transpose(X[0][:, 0:TE4], nat[0:TE4, 0, :], ident[0:TE4, 0:TE4]).then_inc(edge_tr, 1)
            pe.transpose(X[1][:, 0:TE4], nat[0:TE4, 1, :], ident[0:TE4, 0:TE4]).then_inc(edge_tr, 1)
            pe.wait_ge(biases_loaded, 48)
            pe.transpose(X[3][:, 0:NB], b_nat[:, :], ident[0:NB, 0:NB]).then_inc(bias_tr, 1)
            pe.wait_ge(bad_ready, 1)
            pe.matmul(X[2][:, 0:1], ones[0:TE4 - 2, :], bad[0:TE4 - 2, 0:1], start=True, stop=True).then_inc(bad_sum, 1)

            def edge_step(o, q):
                pe.wait_ge(e_lo_ready, o + 1)
                pe.wait_ge(e_link, 6 * o + 2)
                wait(pe, e_sum_ready, o)
                pe.matmul(HB[:, 0:D], e_eq[:, q, 0, :], e_h_hi[:, q, :], start=True, stop=False)
                pe.matmul(HB[:, 0:D], e_eq[:, q, 0, :], e_h_lo[:, q, :], start=False, stop=True).then_inc(e_summed, 1)

            general_case = edges_ahead(pe, nothing, edge_step)

            def transpose_in(n, q):
                pe.wait_ge(h1_ready, n + 1)
                wait(pe, out_ready, n - 2)
                for j in range(SUB):
                    last = pe.transpose(HB[:, j * P:(j + 1) * P], agg_in[:, q, j * D:(j + 1) * D], ident[:, :])
                last.then_inc(hT_ps, 1)

            def layer1(n):
                pe.wait_ge(hT_lo_ready, n + 1)
                for c in range(KC):
                    wait(pe, a3_lo_ready, KC * (n - 2) + c + 1)
                    product(X[c][:, :], lambda a, k: W[1][a][:, c * P:(c + 1) * P], lambda b, k: HT[b][:, :], 1)\
                        .then_inc(l1_ps, 1)

            def step(i, q):
                if isinstance(i, int) and i == 0:
                    pe.wait_ge(w_low, 4)
                    pe.wait_ge(e_sum_ready, E0)
                    transpose_in(0, 0)
                    layer1(0)
                if exists(i + 1):
                    transpose_in(i + 1, 1 - q)
                for c in range(KC):
                    if exists(i):
                        pe.wait_ge(a1_lo_ready, KC * (i + 1))
                        if c < 2:
                            wait(pe, z_copied, SUB * i - 1 + c)
                        else:
                            pe.wait_ge(pre2_ready, KC * i + c - 1)
                        product(Y[c % 2][:, :], lambda a, k: W[2][a][:, k * H + c * P:k * H + (c + 1) * P],
                                lambda b, k: A1[b][:, k, :], KC).then_inc(l2_ps, 1)
                    if exists(i - 1) and c < KC // 2:
                        pe.wait_ge(z_b3_ready, SUB * i)
                        wait(pe, a1_lo_ready, KC * (i + 1) if exists(i) else KC * T)
                        for f in (2 * c, 2 * c + 1):
                            for j in range(SUB):
                                last = pe.transpose(X[f][:, j * P:(j + 1) * P],
                                                    z_b3[:, j * H + f * P:j * H + (f + 1) * P], ident[:, :])
                            last.then_inc(zT_ps, 1)
                if exists(i + 1):
                    layer1(i + 1)
                if exists(i - 1):
                    pe.wait_ge(a3_lo_ready, KC * i)
                    wait(pe, oT_ready, i - 1)
                    product(OB[:, :], lambda a, k: W[4][a][:, k * D:(k + 1) * D], lambda b, k: A3[b][:, k, :], KC)\
                        .then_inc(l4_ps, 1)
                o = i + E0 - 1
                if not isinstance(i, int) or i > 0:
                    edge_part(pe, general_case, edge_step, o, 1 - q)
                for j in range(SUB):
                    if exists(i):
                        pe.wait_ge(h2_lo_ready, KC * (i + 1))
                        if j < 2:
                            pe.wait_ge(pre2_ready, KC * i + j + 3)
                        else:
                            pe.wait_ge(z_copied, SUB * i + j - 1)
                        product(Y[j % 2][:, :], lambda a, k: H2[a][:, k, j * P:(j + 1) * P],
                                lambda b, k: W[3][b][:, k * H:(k + 1) * H], KC).then_inc(z_ps, 1)
                    if j == 1 and exists(i - 1):
                        pe.wait_ge(oT_ready, i)
                        if o_exists(o):
                            pe.wait_ge(e_sum_ready, o + 1)
                        if exists(i + 1):
                            pe.wait_ge(hT_lo_ready, i + 2)
                        for s in range(SUB):
                            last = pe.transpose(HB[:, s * P:(s + 1) * P], oT[:, s * P:(s + 1) * P], ident[:, :])
                        last.then_inc(o_ps, 1)

            node_loop(pe, step)
            tail_pe(pe, product)


_INS = ["x", "src", "dst", "L0_gnn_w1", "L0_gnn_b1", "L0_gnn_w2", "L0_gnn_b2", "L0_gnn_w3", "L0_gnn_b3",
        "L0_gnn_w4", "L0_gnn_b4"]


def kernel(**inputs):
    import numpy as np
    import concourse.bacc as bacc
    from concourse.bass_utils import run_bass_kernel_spmd

    nc = bacc.Bacc("TRN2", target_bir_lowering=False, num_devices=1)
    arrays, args = {}, []
    for name in _INS:
        a = np.ascontiguousarray(inputs[name])
        arrays[f"in_{name}"] = a
        args.append(nc.dram_tensor(f"in_{name}", a.shape, mybir.dt.from_np(a.dtype), kind="ExternalInput").ap())
    args.append(nc.dram_tensor("out_0", inputs["x"].shape, F32, kind="ExternalOutput").ap())
    gnn_kernel(nc, *args)
    r = run_bass_kernel_spmd(nc, [arrays], core_ids=[0])
    return r.results[0]["out_0"]
```
